# Optimizing a Trainium2 kernel written in Bass

```python
import numpy as np
import jax
import jax.numpy as jnp

def _softmax(x, axis=-1):
    return jax.nn.softmax(x, axis=axis)

def _gelu(x):
    return jax.nn.gelu(x, approximate=True)

def _silu(x):
    return jax.nn.silu(x)

def _sigmoid(x):
    return jax.nn.sigmoid(x)

def _layernorm(x, axis=-1, eps=1e-05):
    m = jnp.mean(x, axis=axis, keepdims=True)
    v = jnp.var(x, axis=axis, keepdims=True)
    return (x - m) / jnp.sqrt(v + eps)

def _scatter_add(tgt, idx, src, axis=0):
    return tgt.at[idx].add(src)

def _segment_sum(src, seg, n):
    return jax.ops.segment_sum(src, seg, n)
kernel_name = 'mk_dlrm_tower_d1_rec_r8_5b71e8'

def setup_inputs(seed: int=0):
    np.random.seed(seed)
    _w = jnp.asarray

    def _rec_inputs():
        import jax
        import jax.numpy as jnp
        _tk = jax.random.key(seed)
        dense_ctx = jax.random.normal(jax.random.fold_in(_tk, 190), (512, 16), jnp.float32)
        ids = jnp.stack([jax.random.randint(jax.random.fold_in(_tk, 200 + f), (512,), 0, v, jnp.int32) for f, v in enumerate([1000, 1250, 125000, 1250, 1000, 12500, 1000, 12500, 1250, 1250, 1000, 1250, 1250, 12500, 1250, 12500, 12500, 1250, 12500, 1250, 12500, 1250, 1000, 12500, 1000, 1250, 1000])], axis=1)
        tbl_0 = 0.05 * jax.random.normal(jax.random.fold_in(_tk, 500 + 0), (1000, 128), jnp.float32)
        tbl_1 = 0.05 * jax.random.normal(jax.random.fold_in(_tk, 500 + 1), (1250, 128), jnp.float32)
        tbl_2 = 0.05 * jax.random.normal(jax.random.fold_in(_tk, 500 + 2), (125000, 128), jnp.float32)
        tbl_3 = 0.05 * jax.random.normal(jax.random.fold_in(_tk, 500 + 3), (1250, 128), jnp.float32)
        tbl_4 = 0.05 * jax.random.normal(jax.random.fold_in(_tk, 500 + 4), (1000, 128), jnp.float32)
        tbl_5 = 0.05 * jax.random.normal(jax.random.fold_in(_tk, 500 + 5), (12500, 128), jnp.float32)
        tbl_6 = 0.05 * jax.random.normal(jax.random.fold_in(_tk, 500 + 6), (1000, 128), jnp.float32)
        tbl_7 = 0.05 * jax.random.normal(jax.random.fold_in(_tk, 500 + 7), (12500, 128), jnp.float32)
        tbl_8 = 0.05 * jax.random.normal(jax.random.fold_in(_tk, 500 + 8), (1250, 128), jnp.float32)
        tbl_9 = 0.05 * jax.random.normal(jax.random.fold_in(_tk, 500 + 9), (1250, 128), jnp.float32)
        tbl_10 = 0.05 * jax.random.normal(jax.random.fold_in(_tk, 500 + 10), (1000, 128), jnp.float32)
        tbl_11 = 0.05 * jax.random.normal(jax.random.fold_in(_tk, 500 + 11), (1250, 128), jnp.float32)
        tbl_12 = 0.05 * jax.random.normal(jax.random.fold_in(_tk, 500 + 12), (1250, 128), jnp.float32)
        tbl_13 = 0.05 * jax.random.normal(jax.random.fold_in(_tk, 500 + 13), (12500, 128), jnp.float32)
        tbl_14 = 0.05 * jax.random.normal(jax.random.fold_in(_tk, 500 + 14), (1250, 128), jnp.float32)
        tbl_15 = 0.05 * jax.random.normal(jax.random.fold_in(_tk, 500 + 15), (12500, 128), jnp.float32)
        tbl_16 = 0.05 * jax.random.normal(jax.random.fold_in(_tk, 500 + 16), (12500, 128), jnp.float32)
        tbl_17 = 0.05 * jax.random.normal(jax.random.fold_in(_tk, 500 + 17), (1250, 128), jnp.float32)
        tbl_18 = 0.05 * jax.random.normal(jax.random.fold_in(_tk, 500 + 18), (12500, 128), jnp.float32)
        tbl_19 = 0.05 * jax.random.normal(jax.random.fold_in(_tk, 500 + 19), (1250, 128), jnp.float32)
        tbl_20 = 0.05 * jax.random.normal(jax.random.fold_in(_tk, 500 + 20), (12500, 128), jnp.float32)
        tbl_21 = 0.05 * jax.random.normal(jax.random.fold_in(_tk, 500 + 21), (1250, 128), jnp.float32)
        tbl_22 = 0.05 * jax.random.normal(jax.random.fold_in(_tk, 500 + 22), (1000, 128), jnp.float32)
        tbl_23 = 0.05 * jax.random.normal(jax.random.fold_in(_tk, 500 + 23), (12500, 128), jnp.float32)
        tbl_24 = 0.05 * jax.random.normal(jax.random.fold_in(_tk, 500 + 24), (1000, 128), jnp.float32)
        tbl_25 = 0.05 * jax.random.normal(jax.random.fold_in(_tk, 500 + 25), (1250, 128), jnp.float32)
        tbl_26 = 0.05 * jax.random.normal(jax.random.fold_in(_tk, 500 + 26), (1000, 128), jnp.float32)
        _rk = jax.random.fold_in(_tk, 7)
        W_top1 = 0.0521996 * jax.random.normal(jax.random.fold_in(_tk, 801), (367, 512), jnp.float32)
        W_top2 = 0.0441942 * jax.random.normal(jax.random.fold_in(_tk, 802), (512, 256), jnp.float32)
        W_top3 = 0.0625 * jax.random.normal(jax.random.fold_in(_tk, 803), (256, 1), jnp.float32)
        b_top1 = jnp.zeros((512,), jnp.float32)
        b_top2 = jnp.zeros((256,), jnp.float32)
        return (dense_ctx, ids, tbl_0, tbl_1, tbl_2, tbl_3, tbl_4, tbl_5, tbl_6, tbl_7, tbl_8, tbl_9, tbl_10, tbl_11, tbl_12, tbl_13, tbl_14, tbl_15, tbl_16, tbl_17, tbl_18, tbl_19, tbl_20, tbl_21, tbl_22, tbl_23, tbl_24, tbl_25, tbl_26, W_top1, b_top1, W_top2, b_top2, W_top3)
    dense_ctx, ids, tbl_0, tbl_1, tbl_2, tbl_3, tbl_4, tbl_5, tbl_6, tbl_7, tbl_8, tbl_9, tbl_10, tbl_11, tbl_12, tbl_13, tbl_14, tbl_15, tbl_16, tbl_17, tbl_18, tbl_19, tbl_20, tbl_21, tbl_22, tbl_23, tbl_24, tbl_25, tbl_26, W_top1, b_top1, W_top2, b_top2, W_top3 = _rec_inputs()

    def _L0_rec_setup():
        import jax, jax.numpy as jnp
        import numpy as np

        def _tri_indices(num_feas):
            return np.array([i * num_feas + j for j in range(1, num_feas) for i in range(j)], dtype=np.int32)
        key = jax.random.key(seed)
        batch, num_feas, embed_dim = (2048, 27, 128)
        inputs = jax.random.normal(key, (batch, num_feas, embed_dim), dtype=jnp.float32)
        return {'inputs': inputs, 'num_feas': num_feas}
    _L0_rec_all = _L0_rec_setup()
    _L0_rec_in = {k: v for k, v in _L0_rec_all.items() if k in ()}
    del _L0_rec_all
    return {'dense_ctx': dense_ctx, 'ids': ids, 'tbl_0': tbl_0, 'tbl_1': tbl_1, 'tbl_2': tbl_2, 'tbl_3': tbl_3, 'tbl_4': tbl_4, 'tbl_5': tbl_5, 'tbl_6': tbl_6, 'tbl_7': tbl_7, 'tbl_8': tbl_8, 'tbl_9': tbl_9, 'tbl_10': tbl_10, 'tbl_11': tbl_11, 'tbl_12': tbl_12, 'tbl_13': tbl_13, 'tbl_14': tbl_14, 'tbl_15': tbl_15, 'tbl_16': tbl_16, 'tbl_17': tbl_17, 'tbl_18': tbl_18, 'tbl_19': tbl_19, 'tbl_20': tbl_20, 'tbl_21': tbl_21, 'tbl_22': tbl_22, 'tbl_23': tbl_23, 'tbl_24': tbl_24, 'tbl_25': tbl_25, 'tbl_26': tbl_26, 'W_top1': W_top1, 'b_top1': b_top1, 'W_top2': W_top2, 'b_top2': b_top2, 'W_top3': W_top3}

def reference(dense_ctx, ids, tbl_0, tbl_1, tbl_2, tbl_3, tbl_4, tbl_5, tbl_6, tbl_7, tbl_8, tbl_9, tbl_10, tbl_11, tbl_12, tbl_13, tbl_14, tbl_15, tbl_16, tbl_17, tbl_18, tbl_19, tbl_20, tbl_21, tbl_22, tbl_23, tbl_24, tbl_25, tbl_26, W_top1, b_top1, W_top2, b_top2, W_top3):
    import jax
    import jax.numpy as jnp

    def _L0_rec_ref(inputs, num_feas):
        import jax, jax.numpy as jnp
        import numpy as np

        def _tri_indices(num_feas):
            return np.array([i * num_feas + j for j in range(1, num_feas) for i in range(j)], dtype=np.int32)
        dot = jnp.einsum('bnd,bmd->bnm', inputs, inputs)
        idx = jnp.asarray(_tri_indices(num_feas))
        flat = dot.reshape(inputs.shape[0], num_feas * num_feas)
        return flat[:, idx]
    e = jnp.stack([tbl_0[ids[:, 0]], tbl_1[ids[:, 1]], tbl_2[ids[:, 2]], tbl_3[ids[:, 3]], tbl_4[ids[:, 4]], tbl_5[ids[:, 5]], tbl_6[ids[:, 6]], tbl_7[ids[:, 7]], tbl_8[ids[:, 8]], tbl_9[ids[:, 9]], tbl_10[ids[:, 10]], tbl_11[ids[:, 11]], tbl_12[ids[:, 12]], tbl_13[ids[:, 13]], tbl_14[ids[:, 14]], tbl_15[ids[:, 15]], tbl_16[ids[:, 16]], tbl_17[ids[:, 17]], tbl_18[ids[:, 18]], tbl_19[ids[:, 19]], tbl_20[ids[:, 20]], tbl_21[ids[:, 21]], tbl_22[ids[:, 22]], tbl_23[ids[:, 23]], tbl_24[ids[:, 24]], tbl_25[ids[:, 25]], tbl_26[ids[:, 26]]], axis=1)
    z = _L0_rec_ref(e, 27)
    z = z.reshape(z.shape[0], -1)
    h = jnp.concatenate([z, dense_ctx], axis=1)
    h = jnp.maximum(h @ W_top1 + b_top1, 0.0)
    h = jnp.maximum(h @ W_top2 + b_top2, 0.0)
    y = h @ W_top3
    return y

_drawn_inputs = setup_inputs


def setup_inputs(seed=0):
    import zlib

    import numpy as np

    out = dict(_drawn_inputs(seed))
    spreads = {'b_top1': (0.0, 0.1), 'b_top2': (0.0, 0.1)}
    factors = {}
    for name, (base, spread) in spreads.items():
        noise = np.random.default_rng([zlib.crc32(name.encode()), seed]).standard_normal(out[name].shape)
        drawn = base * np.exp(spread * noise) if base else spread * noise
        out[name] = jnp.asarray(drawn.astype(out[name].dtype))
    for name, factor in factors.items():
        out[name] = (out[name] * factor).astype(out[name].dtype)
    return out
```

```python
from contextlib import ExitStack

import concourse.bass as bass
from concourse import mybir

F32 = mybir.dt.float32
I32 = mybir.dt.int32
U32 = mybir.dt.uint32
ALU = mybir.AluOpType
ACT = mybir.ActivationFunctionType

P = 128
NF = 27
QUADS = 4
QW = P // QUADS
GRP = 4
GROUPS = [(f, min(GRP, NF - f)) for f in range(0, NF, GRP)]
STEPS = 4
BLOCKS = [(u, min(STEPS * u + STEPS - 1, NF - 1)) for u in range((NF + STEPS - 1) // STEPS)]
BASE = [sum(w for _, w in BLOCKS[:u]) for u in range(len(BLOCKS))]
PAIRS = sum(w for _, w in BLOCKS)
ROWS_PER_BUFFER = 2


def dlrm_tower(nc, dense_ctx, ids, tables, w1, b1, w2, b2, w3, out):
    B, ND = dense_ctx.shape
    TILES = B // P
    H1, H2 = w2.shape
    C1, C2 = H1 // P, H2 // P
    K1 = PAIRS + ND + 1
    NG = len(GROUPS)
    NGV = (NG + 1) // 2
    NGA = NG // 2
    NB = len(BLOCKS)
    JH = QW // 2

    with ExitStack() as ctx:
        def sb(name, shape, dt=F32):
            return ctx.enter_context(nc.sbuf_tensor(name, shape, dt))

        def ps(name, shape):
            return ctx.enter_context(nc.psum_tensor(name, shape, F32))

        def sem(name):
            return ctx.enter_context(nc.semaphore(name))

        idx = sb("idx", [P, TILES, NF], I32)
        ident = sb("ident", [P, P])
        rows = sb("rows", [P, ROWS_PER_BUFFER, NF, P])
        feats = sb("feats", [P, P * NF + QW - NF])
        dots = sb("dots", [P, NB * STEPS, QW])
        turned = sb("turned", [P, QUADS, K1])
        pairs = sb("pairs", [K1, STEPS, P])
        wz = sb("wz", [K1, STEPS, H1])
        w2s = sb("w2s", [P, C1, H2])
        w3s = sb("w3s", [P, C2])
        b2s = sb("b2s", [P, C2])
        h1 = sb("h1", [P, C1, P])
        h2 = sb("h2", [P, C2, P])
        y = sb("y", [1, B])

        turn_ps = ps("turn_ps", [P, 2, GRP, P])
        dots_ps = ps("dots_ps", [P, 2, 512])
        turned_ps = ps("turned_ps", [P, 2, STEPS, P])
        pairs_ps = ps("pairs_ps", [P, 2, STEPS, P])
        h1_ps = turned_ps
        h2_ps = pairs_ps
        y_ps = turned_ps[0:1, 0, 0, :]

        ids_in = sem("ids_in")
        ident_zero = sem("ident_zero")
        ident_done = sem("ident_done")
        blank_zero = sem("blank_zero")
        blank_done = sem("blank_done")
        ones_done = sem("ones_done")
        weights_in = sem("weights_in")
        dense_in = sem("dense_in")
        rows_in = [[sem(f"rows_in_{p}_{g}") for g in range(NG)] for p in range(2)]
        rows_used = [sem(f"rows_used_{p}") for p in range(2)]
        feats_dve = sem("feats_dve")
        feats_act = sem("feats_act")
        dots_done = sem("dots_done")
        dots_dve = sem("dots_dve")
        dots_act = sem("dots_act")
        turned_done = sem("turned_done")
        turned_dve = sem("turned_dve")
        turned_act = sem("turned_act")
        pairs_done = sem("pairs_done")
        pairs_dve = sem("pairs_dve")
        pairs_act = sem("pairs_act")
        h1_done = sem("h1_done")
        h1_dve = sem("h1_dve")
        h1_act = sem("h1_act")
        h2_done = sem("h2_done")
        h2_dve = sem("h2_dve")
        h2_act = sem("h2_act")
        y_done = sem("y_done")
        y_copied = sem("y_copied")
        out_done = sem("out_done")

        feats_bf = feats[:, 0:P * NF].rearrange("p (b f) -> p f b", f=NF)
        n_weight_dmas = (NF - 1) + 2 + 3

        block = ctx.enter_context(nc.Block())

        def lift(eng, copy, done, t, g):
            f, n = GROUPS[g]
            if g < 2 and t > 0:
                eng.wait_ge(dots_done, 2 * t)
            copy(feats_bf[:, f:f + n, :], turn_ps[:, g % 2, 0:n, :]).then_inc(done, 1)

        def move_dots(eng, copy, done, t, h):
            eng.wait_ge(dots_done, 2 * t + h + 1)
            if t > 0:
                eng.wait_ge(turned_done, 2 * t)
            src = dots_ps[:, h, 0:JH * NF].rearrange("p (j m) -> p m j", m=NF)
            copy(dots[:, 0:NF, JH * h:JH * h + JH], src).then_inc(done, 1)

        def move_turned(eng, copy, done, t, h):
            eng.wait_ge(turned_done, 2 * t + h + 1)
            if t > 0:
                eng.wait_ge(pairs_done, t)
            for u, w in BLOCKS[STEPS * h:STEPS * h + STEPS]:
                src = turned_ps[:, h, u % STEPS, :].rearrange("p (q n) -> p q n", q=QUADS)
                last = copy(turned[:, :, BASE[u]:BASE[u] + w], src[:, :, 0:w])
            last.then_inc(done, 1)

        def move_pairs(eng, copy, done, t, h):
            eng.wait_ge(pairs_done, t + 1)
            if t > 0:
                eng.wait_ge(h1_done, 2 * t)
            src = pairs_ps[0:K1, h, 0:2, :].rearrange("k q (v j) -> k v q j", v=STEPS)
            dst = pairs[:, :, 2 * h * QW:(2 * h + 2) * QW].rearrange("k v (q j) -> k v q j", q=2)
            copy(dst, src).then_inc(done, 1)

        @block.sync
        def _(sp):
            sp.dma_start(idx[:], ids.rearrange("(t p) f -> p t f", p=P)).then_inc(ids_in, 16)
            sp.wait_ge(blank_done, 1)
            for m in range(1, NF):
                u, v = m // STEPS, m % STEPS
                first = m * (m - 1) // 2
                sp.dma_start(wz[BASE[u]:BASE[u] + m, v, :], w1[first:first + m, :]).then_inc(weights_in, 16)
            first = NF * (NF - 1) // 2
            sp.dma_start(wz[PAIRS:PAIRS + ND, 0, :], w1[first:first + ND, :]).then_inc(weights_in, 16)
            sp.dma_start(wz[PAIRS + ND:K1, 0, :], b1.rearrange("(a h) -> a h", a=1)).then_inc(weights_in, 16)
            sp.dma_start(w2s[:], w2.rearrange("(c p) h -> p c h", p=P)).then_inc(weights_in, 16)
            with nc.allow_non_contiguous_dma(reason="256 words each, once"):
                sp.dma_start(w3s[:], w3.rearrange("(c p) o -> p (c o)", p=P)).then_inc(weights_in, 16)
                sp.dma_start(b2s[:], b2.rearrange("(c p) -> p c", p=P)).then_inc(weights_in, 16)
            sp.wait_ge(ones_done, 1)
            dense = dense_ctx.rearrange("(t q j) e -> t j q e", q=QUADS, j=QW)
            for t in range(TILES):
                if t > 0:
                    sp.wait_ge(pairs_done, t)
                sp.dma_start(turned[0:QW, :, PAIRS:PAIRS + ND],
                             dense[t]).then_inc(dense_in, 16)
            sp.wait_ge(y_copied, TILES)
            sp.dma_start(out.rearrange("b o -> o b"), y[:]).then_inc(out_done, 16)
            sp.wait_ge(out_done, 16)

        @block.gpsimd
        def _(pool):
            nc.gpsimd.memset(ident[:], 0.0).then_inc(ident_zero, 1)
            pool.wait_ge(ident_zero, 1)
            nc.gpsimd.affine_select(out=ident[:], in_=ident[:], compare_op=ALU.not_equal, fill=1.0, base=0,
                                    pattern=[[-1, P]], channel_multiplier=1).then_inc(ident_done, 1)
            pool.wait_ge(ids_in, 16)
            for t in range(TILES):
                i, p = t // 2, t % 2
                if i > 0:
                    pool.wait_ge(rows_used[p], NG * i)
                for g, (f0, n) in enumerate(GROUPS):
                    for f in range(f0, f0 + n):
                        nc.gpsimd.indirect_dma_start(
                            rows[:, p, f, :], None, tables[f],
                            bass.IndirectOffsetOnAxis(ap=idx[:, t, f:f + 1].bitcast(U32), axis=0),
                        ).then_inc(rows_in[p][g], 16)

        @block.tensor
        def _(pe):
            def turn(t):
                i, p = t // 2, t % 2
                for g, (f, n) in enumerate(GROUPS):
                    pe.wait_ge(rows_in[p][g], (i + 1) * (16 * n))
                    lifted = NGV * t + g // 2 if g % 2 == 0 else NGA * t + g // 2
                    if lifted > 0:
                        pe.wait_ge((feats_dve, feats_act)[g % 2], lifted)
                    for k in range(n):
                        last = nc.tensor.transpose(turn_ps[:, g % 2, k, :], rows[:, p, f + k, :], ident[:])
                    last.then_inc(rows_used[p], 1)

            def gram(t):
                pe.wait_ge(feats_dve, NGV * (t + 1))
                pe.wait_ge(feats_act, NGA * (t + 1))
                for h in range(2):
                    if t > 0:
                        pe.wait_ge((dots_dve, dots_act)[h], t)
                    for j in range(JH * h, JH * h + JH):
                        at = (j - JH * h) * NF
                        for q in range(QUADS):
                            b = (q * QW + j) * NF
                            last = nc.tensor.matmul(dots_ps[q * QW:(q + 1) * QW, h, at:at + NF],
                                                    feats[:, b:b + QW], feats[:, b:b + NF], start=True, stop=True)
                    last.then_inc(dots_done, 1)

            def pair(t):
                pe.wait_ge(dots_dve, t + 1)
                pe.wait_ge(dots_act, t + 1)
                for h in range(2):
                    if h == 0 and t > 0:
                        pe.wait_ge(y_copied, t)
                    for u, _ in BLOCKS[STEPS * h:STEPS * h + STEPS]:
                        src = dots[:, STEPS * u:STEPS * u + STEPS, :].rearrange("p v j -> p (v j)")
                        last = nc.tensor.transpose(turned_ps[:, h, u % STEPS, :], src, ident[:])
                    last.then_inc(turned_done, 1)
                pe.wait_ge(turned_dve, t + 1)
                pe.wait_ge(turned_act, t + 1)
                pe.wait_ge(dense_in, (t + 1) * 16)
                for q in range(QUADS):
                    last = nc.tensor.transpose(pairs_ps[0:K1, q // 2, q % 2, :], turned[:, q, :], ident[:])
                last.then_inc(pairs_done, 1)

            def top(t):
                pe.wait_ge(pairs_dve, t + 1)
                pe.wait_ge(pairs_act, t + 1)
                for c in range(C1):
                    for v in range(STEPS):
                        k = K1 if v == 0 else PAIRS
                        last = nc.tensor.matmul(h1_ps[:, c // (C1 // 2), c % (C1 // 2), :], wz[0:k, v, c * P:(c + 1) * P], pairs[0:k, v, :],
                                                start=(v == 0), stop=(v == STEPS - 1))
                    if (c + 1) % (C1 // 2) == 0:
                        last.then_inc(h1_done, 1)
                pe.wait_ge(h1_dve, t + 1)
                pe.wait_ge(h1_act, t + 1)
                for c in range(C2):
                    for k in range(C1):
                        last = nc.tensor.matmul(h2_ps[:, c, 0, :], w2s[:, k, c * P:(c + 1) * P], h1[:, k, :],
                                                start=(k == 0), stop=(k == C1 - 1))
                    last.then_inc(h2_done, 1)
                pe.wait_ge(h2_dve, t + 1)
                pe.wait_ge(h2_act, t + 1)
                for k in range(C2):
                    last = nc.tensor.matmul(y_ps, w3s[:, k:k + 1], h2[:, k, :], start=(k == 0), stop=(k == C2 - 1))
                last.then_inc(y_done, 1)

            pe.wait_ge(ident_done, 1)
            pe.wait_ge(blank_done, 1)
            pe.wait_ge(ones_done, 1)
            for t in range(TILES):
                turn(t)
                gram(t)
                pair(t)
                if t == 0:
                    pe.wait_ge(weights_in, 16 * n_weight_dmas)
                top(t)

        @block.vector
        def _(dve):
            nc.vector.memset(feats[:, P * NF:], 0.0)
            nc.vector.memset(dots[:, NF:, :], 0.0)
            nc.vector.memset(turned[:, :, PAIRS:], 0.0).then_inc(blank_zero, 1)
            nc.vector.memset(wz[:], 0.0).then_inc(blank_done, 1)
            dve.wait_ge(blank_zero, 1)
            nc.vector.memset(turned[0:QW, :, PAIRS + ND:], 1.0).then_inc(ones_done, 1)
            for i in range(TILES // 2):
                for p in range(2):
                    t = 2 * i + p
                    for g in range(0, NG, 2):
                        dve.wait_ge(rows_used[p], NG * i + g + 1)
                        lift(dve, nc.vector.tensor_copy, feats_dve, t, g)
                    move_dots(dve, nc.vector.tensor_copy, dots_dve, t, 0)
                    move_turned(dve, nc.vector.tensor_copy, turned_dve, t, 0)
                    move_pairs(dve, nc.vector.tensor_copy, pairs_dve, t, 0)
                    dve.wait_ge(h1_done, 2 * t + 1)
                    if t > 0:
                        dve.wait_ge(h2_done, 2 * t)
                    nc.vector.tensor_scalar_max(h1[:, 0:C1 // 2, :], h1_ps[:, 0, 0:C1 // 2, :], 0.0).then_inc(h1_dve, 1)
                    dve.wait_ge(h2_done, 2 * t + 1)
                    if t > 0:
                        dve.wait_ge(y_done, t)
                    nc.vector.tensor_scalar(h2[:, 0, :], h2_ps[:, 0, 0, :], b2s[:, 0:1], 0.0,
                                            ALU.add, ALU.max).then_inc(h2_dve, 1)
                    dve.wait_ge(y_done, t + 1)
                    nc.vector.tensor_copy(y[:, bass.ts(t, P)], y_ps).then_inc(y_copied, 1)

        @block.scalar
        def _(act):
            act.wait_ge(weights_in, 16 * n_weight_dmas)
            for i in range(TILES // 2):
                for p in range(2):
                    t = 2 * i + p
                    for g in range(1, NG, 2):
                        act.wait_ge(rows_used[p], NG * i + g + 1)
                        lift(act, nc.scalar.copy, feats_act, t, g)
                    move_dots(act, nc.scalar.copy, dots_act, t, 1)
                    move_turned(act, nc.scalar.copy, turned_act, t, 1)
                    move_pairs(act, nc.scalar.copy, pairs_act, t, 1)
                    act.wait_ge(h1_done, 2 * t + 2)
                    if t > 0:
                        act.wait_ge(h2_done, 2 * t)
                    nc.scalar.activation(h1[:, C1 // 2:, :], h1_ps[:, 1, 0:C1 // 2, :], ACT.Relu).then_inc(h1_act, 1)
                    act.wait_ge(h2_done, 2 * t + 2)
                    if t > 0:
                        act.wait_ge(y_done, t)
                    nc.scalar.activation(h2[:, 1, :], h2_ps[:, 1, 0, :], ACT.Relu,
                                         bias=b2s[:, 1:2]).then_inc(h2_act, 1)


def kernel(**inputs):
    import numpy as np
    import concourse.bacc as bacc
    from concourse.bass_utils import run_bass_kernel_spmd

    nc = bacc.Bacc("TRN2", target_bir_lowering=False, num_devices=1)
    arrays, dram = {}, {}
    for name, a in inputs.items():
        a = np.ascontiguousarray(a)
        arrays[f"in_{name}_dram"] = a
        dram[name] = nc.dram_tensor(f"in_{name}_dram", a.shape, mybir.dt.from_np(a.dtype), kind="ExternalInput").ap()
    batch = inputs["ids"].shape[0]
    out = nc.dram_tensor("out_0_dram", (batch, 1), F32, kind="ExternalOutput").ap()
    dlrm_tower(nc, dram["dense_ctx"], dram["ids"], [dram[f"tbl_{f}"] for f in range(NF)], dram["W_top1"],
               dram["b_top1"], dram["W_top2"], dram["b_top2"], dram["W_top3"], out)
    r = run_bass_kernel_spmd(nc, [arrays], core_ids=[0])
    return r.results[0]["out_0_dram"]
```

```python
from contextlib import ExitStack

import concourse.bass as bass
from concourse import mybir

F32 = mybir.dt.float32
F16 = mybir.dt.float16
BF16 = mybir.dt.bfloat16
I32 = mybir.dt.int32
U32 = mybir.dt.uint32
ALU = mybir.AluOpType
ACT = mybir.ActivationFunctionType

P = 128
NF = 27
SELECTED = [0, 4, 6, 10, 22, 24, 26]
GATHERED = [f for f in range(NF) if f not in SELECTED]
ORDER = GATHERED + SELECTED
NS = len(SELECTED)
NGA = len(GATHERED)
RP = 125
RP_EVEN = 112
QUADS = 4
QW = P // QUADS
GRP = 4
GROUPS = [(f, min(GRP, NGA - f)) for f in range(0, NGA, GRP)]
NG = len(GROUPS)
EARLY = 2 * NG
STEPS = 4
BLOCKS = [(u, min(STEPS * u + STEPS - 1, NF - 1)) for u in range((NF + STEPS - 1) // STEPS)]
NB = len(BLOCKS)
BASE = [sum(w for _, w in BLOCKS[:u]) for u in range(NB)]
PAIRS = sum(w for _, w in BLOCKS)
JH = QW // 2
PARTS = 3


def dlrm_tower(nc, dense_ctx, ids, tables, w1_steps, w2, b2, w3, out):
    B, ND = dense_ctx.shape
    TILES = B // P
    H1, H2 = w2.shape
    C1, C2 = H1 // P, H2 // P
    K1 = PAIRS + ND + 1
    CH = [tables[f].shape[0] // RP for f in SELECTED]
    CMAX = max(CH)

    with ExitStack() as ctx:
        def sb(name, shape, dt=F32):
            return ctx.enter_context(nc.sbuf_tensor(name, shape, dt))

        def ps(name, shape):
            return ctx.enter_context(nc.psum_tensor(name, shape, F32))

        def sem(name):
            return ctx.enter_context(nc.semaphore(name))

        idx = sb("idx", [P, TILES, NF], I32)
        ident = sb("ident", [P, P])
        ident16 = sb("ident16", [P, P], F16)
        row_no_int = {c: sb(f"row_no_int_{c}", [P, c], I32) for c in sorted(set(CH))}
        row_no = {c: sb(f"row_no_{c}", [P, c]) for c in row_no_int}
        wide_ids = sb("wide_ids", [P, 2, TILES, P], F16)
        stage = sb("stage", [P, 3, CMAX * P])
        part = sb("part", [P, 3, PARTS, CMAX * P], BF16)
        hot = sb("hot", [P, 2, CMAX, B], BF16)
        rows = sb("rows", [P, TILES, NGA, P])
        feats = sb("feats", [P, TILES, P * NF + QW - NF])
        dots = sb("dots", [P, NB * STEPS, QW])
        turned = sb("turned", [P, QUADS, K1])
        pairs = sb("pairs", [K1, STEPS, P])
        w1s = sb("w1s", [K1, STEPS, H1])
        w2s = sb("w2s", [P, C1, H2])
        w3s = sb("w3s", [P, C2])
        b2s = sb("b2s", [P, C2])
        h1 = sb("h1", [P, C1, P])
        h2 = sb("h2", [P, C2, P])
        y = sb("y", [1, B])

        turn_ps = ps("turn_ps", [P, 2, GRP, P])
        dots_ps = ps("dots_ps", [P, 2, 512])
        turned_ps = ps("turned_ps", [P, 2, STEPS, P])
        pairs_ps = ps("pairs_ps", [P, 2, STEPS, P])
        h1_ps = turned_ps
        h2_ps = pairs_ps
        y_ps = pairs_ps[0:1, 0, 1, :]
        wide_ps = [turned_ps[:, k].rearrange("p a b -> p (a b)").bitcast(F16)[:, 0:B] for k in range(2)]
        select_ps = [pairs_ps[:, k].rearrange("p a b -> p (a b)") for k in range(2)]

        ids_in = sem("ids_in")
        ident_zero = sem("ident_zero")
        ident_done = sem("ident_done")
        ident16_done = sem("ident16_done")
        row_no_int_done = sem("row_no_int_done")
        row_no_done = sem("row_no_done")
        blank_done = sem("blank_done")
        ones_done = sem("ones_done")
        table_in = [sem(f"table_in_{k}") for k in range(3)]
        weights_in = sem("weights_in")
        dense_in = sem("dense_in")
        rows_in = [[sem(f"rows_in_{t}_{g}") for g in range(NG)] for t in range(TILES)]
        wide_done = sem("wide_done")
        spread_done = sem("spread_done")
        hot_done = sem("hot_done")
        high_done = sem("high_done")
        rest_done = sem("rest_done")
        mid_done = sem("mid_done")
        low_done = sem("low_done")
        select_done = sem("select_done")
        feats_sel = sem("feats_sel")
        turn_done = sem("turn_done")
        feats_dve = sem("feats_dve")
        feats_act = sem("feats_act")
        dots_done = sem("dots_done")
        dots_dve = sem("dots_dve")
        dots_act = sem("dots_act")
        turned_done = sem("turned_done")
        turned_dve = sem("turned_dve")
        turned_act = sem("turned_act")
        pairs_done = sem("pairs_done")
        pairs_dve = sem("pairs_dve")
        pairs_act = sem("pairs_act")
        h1_done = sem("h1_done")
        h1_dve = sem("h1_dve")
        h1_act = sem("h1_act")
        h2_done = sem("h2_done")
        h2_dve = sem("h2_dve")
        h2_act = sem("h2_act")
        y_done = sem("y_done")
        y_copied = sem("y_copied")
        out_done = sem("out_done")

        feats_fb = feats[:, :, 0:P * NF].rearrange("p t (b f) -> p f t b", f=NF)
        N_WEIGHTS = 4

        def lifter(n):
            if n < EARLY:
                return feats_act, n + 1
            late = n - EARLY
            return (feats_dve, late // 2 + 1) if late % 2 == 0 else (feats_act, EARLY + late // 2 + 1)

        def lift(eng, copy, n):
            t, (f, m) = n // NG, GROUPS[n % NG]
            eng.wait_ge(turn_done, n + 1)
            copy(feats_fb[:, f:f + m, t, :], turn_ps[:, n % 2, 0:m, :]).then_inc(lifter(n)[0], 1)

        def move_dots(eng, copy, done, t, h):
            eng.wait_ge(dots_done, 2 * t + h + 1)
            if t > 0:
                eng.wait_ge(turned_done, 2 * t)
            src = dots_ps[:, h, 0:JH * NF].rearrange("p (j m) -> p m j", m=NF)
            copy(dots[:, 0:NF, JH * h:JH * h + JH], src).then_inc(done, 1)

        def move_turned(eng, copy, done, t, h):
            eng.wait_ge(turned_done, 2 * t + h + 1)
            if t > 0:
                eng.wait_ge(pairs_done, 2 * t)
            for u, w in BLOCKS[STEPS * h:STEPS * h + STEPS]:
                src = turned_ps[:, h, u % STEPS, :].rearrange("p (q n) -> p q n", q=QUADS)
                last = copy(turned[:, :, BASE[u]:BASE[u] + w], src[:, :, 0:w])
            last.then_inc(done, 1)

        def move_pairs(eng, copy, done, t, h):
            eng.wait_ge(pairs_done, 2 * t + h + 1)
            if t > 0:
                eng.wait_ge(h1_done, 2 * t)
            src = pairs_ps[0:K1, h, 0:2, :].rearrange("k q (v j) -> k v q j", v=STEPS)
            dst = pairs[:, :, 2 * h * QW:(2 * h + 2) * QW].rearrange("k v (q j) -> k v q j", q=2)
            copy(dst, src).then_inc(done, 1)

        block = ctx.enter_context(nc.Block())

        @block.sync
        def _(sp):
            sp.dma_start(idx[:], ids.rearrange("(t p) f -> p t f", p=P)).then_inc(ids_in, 16)
            for k, f in enumerate(SELECTED):
                if k >= 3:
                    sp.wait_ge(low_done, k - 2)
                table = tables[f].rearrange("(p c) d -> p (c d)", p=RP)
                n = CH[k] * P
                for p0, p1 in ((0, RP_EVEN), (RP_EVEN, RP)):
                    sp.dma_start(stage[p0:p1, k % 3, 0:n], table[p0:p1, :]).then_inc(table_in[k % 3], 16)
            sp.dma_start(w1s[:], w1_steps).then_inc(weights_in, 16)
            sp.dma_start(w2s[:], w2.rearrange("(c p) h -> p c h", p=P)).then_inc(weights_in, 16)
            with nc.allow_non_contiguous_dma(reason="256 words each, once"):
                sp.dma_start(w3s[:], w3.rearrange("(c p) o -> p (c o)", p=P)).then_inc(weights_in, 16)
                sp.dma_start(b2s[:], b2.rearrange("(c p) -> p c", p=P)).then_inc(weights_in, 16)
            sp.wait_ge(ones_done, 1)
            dense = dense_ctx.rearrange("(t q j) e -> t j q e", q=QUADS, j=QW)
            for t in range(TILES):
                if t > 0:
                    sp.wait_ge(pairs_done, 2 * t)
                sp.dma_start(turned[0:QW, :, PAIRS:PAIRS + ND], dense[t]).then_inc(dense_in, 16)
            sp.wait_ge(y_copied, TILES)
            sp.dma_start(out.rearrange("b o -> o b"), y[:]).then_inc(out_done, 16)
            sp.wait_ge(out_done, 16)

        @block.gpsimd
        def _(pool):
            nc.gpsimd.memset(ident[:], 0.0).then_inc(ident_zero, 1)
            pool.wait_ge(ident_zero, 1)
            nc.gpsimd.affine_select(out=ident[:], in_=ident[:], compare_op=ALU.not_equal, fill=1.0, base=0,
                                    pattern=[[-1, P]], channel_multiplier=1).then_inc(ident_done, 1)
            for c in row_no:
                nc.gpsimd.iota(row_no_int[c][:], pattern=[[1, c]], base=0,
                               channel_multiplier=c).then_inc(row_no_int_done, 1)
            pool.wait_ge(ids_in, 16)
            for t in range(TILES):
                for g, (f0, n) in enumerate(GROUPS):
                    for i in range(f0, f0 + n):
                        f = GATHERED[i]
                        nc.gpsimd.indirect_dma_start(
                            rows[:, t, i, :], None, tables[f],
                            bass.IndirectOffsetOnAxis(ap=idx[:, t, f:f + 1].bitcast(U32), axis=0),
                        ).then_inc(rows_in[t][g], 16)

        @block.tensor
        def _(pe):
            def spread(k):
                pe.wait_ge(wide_done, k + 1)
                if k >= 2:
                    pe.wait_ge(hot_done, 2 * (k - 1))
                for t in range(TILES):
                    last = nc.tensor.transpose(wide_ps[k % 2][0:RP, t * P:(t + 1) * P], wide_ids[:, k % 2, t, 0:RP],
                                               ident16[:])
                last.then_inc(spread_done, 1)

            def select(k):
                if k >= 2:
                    pe.wait_ge(feats_sel, k - 1)
                for s in range(PARTS):
                    pe.wait_ge((high_done, mid_done, low_done)[s], k + 1)
                    for c in range(CH[k]):
                        if s == 0 and c == 0:
                            pe.wait_ge(hot_done, 2 * k + 1)
                        if s == 0 and c == CH[k] // 2:
                            pe.wait_ge(hot_done, 2 * k + 2)
                        last = nc.tensor.matmul(select_ps[k % 2], part[0:RP, k % 3, s, c * P:(c + 1) * P],
                                                hot[0:RP, k % 2, c, :], start=(s == 0 and c == 0),
                                                stop=(s == PARTS - 1 and c == CH[k] - 1))
                last.then_inc(select_done, 1)

            def turn(n):
                t, (f, m) = n // NG, GROUPS[n % NG]
                pe.wait_ge(rows_in[t][n % NG], 16 * m)
                if n >= 2:
                    pe.wait_ge(*lifter(n - 2))
                for i in range(m):
                    last = nc.tensor.transpose(turn_ps[:, n % 2, i, :], rows[:, t, f + i, :], ident[:])
                last.then_inc(turn_done, 1)

            def gram(t, h):
                pe.wait_ge(feats_sel, NS)
                pe.wait_ge(*lifter(NG * t + NG - 2))
                pe.wait_ge(*lifter(NG * t + NG - 1))
                if t > 0:
                    pe.wait_ge((dots_dve, dots_act)[h], t)
                for j in range(JH * h, JH * h + JH):
                    at = (j - JH * h) * NF
                    for q in range(QUADS):
                        b = (q * QW + j) * NF
                        last = nc.tensor.matmul(dots_ps[q * QW:(q + 1) * QW, h, at:at + NF],
                                                feats[:, t, b:b + QW], feats[:, t, b:b + NF], start=True, stop=True)
                last.then_inc(dots_done, 1)

            def turn_dots(t):
                pe.wait_ge(dots_dve, t + 1)
                pe.wait_ge(dots_act, t + 1)
                for h in range(2):
                    if t > 0:
                        pe.wait_ge((h1_dve, h1_act)[h], t)
                    for u, _ in BLOCKS[STEPS * h:STEPS * h + STEPS]:
                        src = dots[:, STEPS * u:STEPS * u + STEPS, :].rearrange("p v j -> p (v j)")
                        last = nc.tensor.transpose(turned_ps[:, h, u % STEPS, :], src, ident[:])
                    last.then_inc(turned_done, 1)

            def turn_pairs(t):
                pe.wait_ge(turned_dve, t + 1)
                pe.wait_ge(turned_act, t + 1)
                pe.wait_ge(dense_in, (t + 1) * 16)
                if t > 0:
                    pe.wait_ge(y_copied, t)
                for h in range(2):
                    if t > 0:
                        pe.wait_ge((h2_dve, h2_act)[h], t)
                    for q in (2 * h, 2 * h + 1):
                        last = nc.tensor.transpose(pairs_ps[0:K1, h, q % 2, :], turned[:, q, :], ident[:])
                    last.then_inc(pairs_done, 1)

            def layer1(t):
                pe.wait_ge(pairs_dve, t + 1)
                pe.wait_ge(pairs_act, t + 1)
                for c in range(C1):
                    for v in range(STEPS):
                        k = K1 if v == 0 else PAIRS
                        last = nc.tensor.matmul(h1_ps[:, c // (C1 // 2), c % (C1 // 2), :],
                                                w1s[0:k, v, c * P:(c + 1) * P], pairs[0:k, v, :],
                                                start=(v == 0), stop=(v == STEPS - 1))
                    if (c + 1) % (C1 // 2) == 0:
                        last.then_inc(h1_done, 1)

            def layer2(t):
                for half in range(2):
                    pe.wait_ge((h1_dve, h1_act)[half], t + 1)
                    for c in range(C2):
                        for k in range(half * C1 // 2, (half + 1) * C1 // 2):
                            last = nc.tensor.matmul(h2_ps[:, c, 0, :], w2s[:, k, c * P:(c + 1) * P], h1[:, k, :],
                                                    start=(k == 0), stop=(k == C1 - 1))
                        if half == 1:
                            last.then_inc(h2_done, 1)

            def layer3(t):
                pe.wait_ge(h2_dve, t + 1)
                pe.wait_ge(h2_act, t + 1)
                for k in range(C2):
                    last = nc.tensor.matmul(y_ps, w3s[:, k:k + 1], h2[:, k, :], start=(k == 0), stop=(k == C2 - 1))
                last.then_inc(y_done, 1)

            pe.wait_ge(ident16_done, 1)
            spread(0)
            pe.wait_ge(ident_done, 1)
            for k in range(NS):
                if k + 1 < NS:
                    spread(k + 1)
                select(k)
                for n in range((EARLY - 1) * k // NS, (EARLY - 1) * (k + 1) // NS):
                    turn(n)
            pe.wait_ge(blank_done, 1)
            pe.wait_ge(ones_done, 1)
            pe.wait_ge(weights_in, 16 * N_WEIGHTS)
            gram(0, 0)
            gram(0, 1)
            turn(EARLY - 1)
            turn_dots(0)
            gram(1, 0)
            turn_pairs(0)
            gram(1, 1)
            layer1(0)
            turn_dots(1)
            turn(2 * NG)
            layer2(0)
            turn(2 * NG + 1)
            layer3(0)
            turn(2 * NG + 2)
            turn_pairs(1)
            turn(2 * NG + 3)
            layer1(1)
            turn(2 * NG + 4)
            layer2(1)
            gram(2, 0)
            layer3(1)
            gram(2, 1)
            turn(3 * NG)
            turn_dots(2)
            turn(3 * NG + 1)
            turn_pairs(2)
            turn(3 * NG + 2)
            layer1(2)
            turn(3 * NG + 3)
            turn(3 * NG + 4)
            layer2(2)
            gram(3, 0)
            gram(3, 1)
            layer3(2)
            turn_dots(3)
            turn_pairs(3)
            layer1(3)
            layer2(3)
            layer3(3)

        @block.vector
        def _(dve):
            copy = nc.vector.tensor_copy

            def rest(k):
                dve.wait_ge(high_done, k + 1)
                n = CH[k] * P
                nc.vector.tensor_tensor(stage[0:RP, k % 3, 0:n], stage[0:RP, k % 3, 0:n], part[0:RP, k % 3, 0, 0:n],
                                        ALU.subtract).then_inc(rest_done, 1)

            def low(k):
                dve.wait_ge(mid_done, k + 1)
                n = CH[k] * P
                nc.vector.tensor_tensor(part[0:RP, k % 3, 2, 0:n], stage[0:RP, k % 3, 0:n], part[0:RP, k % 3, 1, 0:n],
                                        ALU.subtract).then_inc(low_done, 1)

            def one_hot(k, h):
                if h == 0:
                    dve.wait_ge(spread_done, k + 1)
                    if k >= 2:
                        dve.wait_ge(select_done, k - 1)
                half = CH[k] // 2
                for c in range(h * half, h * half + half):
                    last = nc.vector.tensor_scalar(hot[0:RP, k % 2, c, :], wide_ps[k % 2][0:RP, :],
                                                   row_no[CH[k]][0:RP, c:c + 1], None, ALU.is_equal)
                last.then_inc(hot_done, 1)

            def relu1(t):
                dve.wait_ge(h1_done, 2 * t + 1)
                nc.vector.tensor_scalar_max(h1[:, 0:C1 // 2, :], h1_ps[:, 0, 0:C1 // 2, :], 0.0).then_inc(h1_dve, 1)

            def relu2(t):
                dve.wait_ge(h2_done, 2 * t + 1)
                nc.vector.tensor_scalar(h2[:, 0, :], h2_ps[:, 0, 0, :], b2s[:, 0:1], 0.0,
                                        ALU.add, ALU.max).then_inc(h2_dve, 1)

            def copy_y(t):
                dve.wait_ge(y_done, t + 1)
                copy(y[:, t * P:(t + 1) * P], y_ps).then_inc(y_copied, 1)

            nc.vector.memset(feats[:, :, P * NF:], 0.0)
            nc.vector.memset(dots[:, NF:, :], 0.0)
            nc.vector.memset(turned[:, :, PAIRS:], 0.0).then_inc(blank_done, 1)
            dve.wait_ge(ident_done, 1)
            copy(ident16[:], ident[:]).then_inc(ident16_done, 1)
            dve.wait_ge(blank_done, 1)
            nc.vector.memset(turned[0:QW, :, PAIRS + ND:], 1.0).then_inc(ones_done, 1)
            dve.wait_ge(row_no_int_done, len(row_no))
            for c in row_no:
                copy(row_no[c][:], row_no_int[c][:]).then_inc(row_no_done, 1)
            dve.wait_ge(row_no_done, len(row_no))
            for k in range(NS):
                if k == 0:
                    one_hot(0, 0)
                    one_hot(0, 1)
                    rest(0)
                    low(0)
                else:
                    rest(k)
                    one_hot(k, 0)
                    low(k)
                    one_hot(k, 1)
            move_dots(dve, copy, dots_dve, 0, 0)
            move_turned(dve, copy, turned_dve, 0, 0)
            move_dots(dve, copy, dots_dve, 1, 0)
            move_pairs(dve, copy, pairs_dve, 0, 0)
            relu1(0)
            move_turned(dve, copy, turned_dve, 1, 0)
            lift(dve, copy, 2 * NG)
            relu2(0)
            copy_y(0)
            lift(dve, copy, 2 * NG + 2)
            move_pairs(dve, copy, pairs_dve, 1, 0)
            relu1(1)
            lift(dve, copy, 2 * NG + 4)
            relu2(1)
            move_dots(dve, copy, dots_dve, 2, 0)
            copy_y(1)
            move_turned(dve, copy, turned_dve, 2, 0)
            lift(dve, copy, 3 * NG + 1)
            move_pairs(dve, copy, pairs_dve, 2, 0)
            relu1(2)
            lift(dve, copy, 3 * NG + 3)
            relu2(2)
            move_dots(dve, copy, dots_dve, 3, 0)
            copy_y(2)
            move_turned(dve, copy, turned_dve, 3, 0)
            move_pairs(dve, copy, pairs_dve, 3, 0)
            relu1(3)
            relu2(3)
            copy_y(3)

        @block.scalar
        def _(act):
            copy = nc.scalar.copy

            def widen(k):
                if k >= 2:
                    act.wait_ge(spread_done, k - 1)
                f = SELECTED[k]
                copy(wide_ids[:, k % 2, :, :], idx[:, :, f:f + 1].to_broadcast([P, TILES, P])).then_inc(wide_done, 1)

            def high(k):
                act.wait_ge(table_in[k % 3], 32 * (k // 3 + 1))
                if k >= 3:
                    act.wait_ge(select_done, k - 2)
                n = CH[k] * P
                copy(part[0:RP, k % 3, 0, 0:n], stage[0:RP, k % 3, 0:n]).then_inc(high_done, 1)

            def mid(k):
                act.wait_ge(rest_done, k + 1)
                n = CH[k] * P
                copy(part[0:RP, k % 3, 1, 0:n], stage[0:RP, k % 3, 0:n]).then_inc(mid_done, 1)

            def lift_selected(k):
                act.wait_ge(select_done, k + 1)
                copy(feats_fb[:, NGA + k, :, :], select_ps[k % 2].rearrange("p (t b) -> p t b", t=TILES)).then_inc(feats_sel, 1)

            def lift_round(k):
                lift_selected(k)
                for n in range((EARLY - 1) * k // NS, (EARLY - 1) * (k + 1) // NS):
                    lift(act, copy, n)

            def relu1(t):
                act.wait_ge(h1_done, 2 * t + 2)
                nc.scalar.activation(h1[:, C1 // 2:, :], h1_ps[:, 1, 0:C1 // 2, :], ACT.Relu).then_inc(h1_act, 1)

            def relu2(t):
                act.wait_ge(h2_done, 2 * t + 2)
                nc.scalar.activation(h2[:, 1, :], h2_ps[:, 1, 0, :], ACT.Relu, bias=b2s[:, 1:2]).then_inc(h2_act, 1)

            act.wait_ge(ids_in, 16)
            widen(0)
            for k in range(NS):
                if k + 1 < NS:
                    widen(k + 1)
                high(k)
                mid(k)
                if k >= 2:
                    lift_round(k - 2)
            lift_round(NS - 2)
            lift_round(NS - 1)
            move_dots(act, copy, dots_act, 0, 1)
            lift(act, copy, EARLY - 1)
            move_turned(act, copy, turned_act, 0, 1)
            move_pairs(act, copy, pairs_act, 0, 1)
            move_dots(act, copy, dots_act, 1, 1)
            act.wait_ge(weights_in, 16 * N_WEIGHTS)
            relu1(0)
            move_turned(act, copy, turned_act, 1, 1)
            relu2(0)
            lift(act, copy, 2 * NG + 1)
            move_pairs(act, copy, pairs_act, 1, 1)
            lift(act, copy, 2 * NG + 3)
            relu1(1)
            relu2(1)
            move_dots(act, copy, dots_act, 2, 1)
            lift(act, copy, 3 * NG)
            move_turned(act, copy, turned_act, 2, 1)
            move_pairs(act, copy, pairs_act, 2, 1)
            lift(act, copy, 3 * NG + 2)
            relu1(2)
            lift(act, copy, 3 * NG + 4)
            relu2(2)
            move_dots(act, copy, dots_act, 3, 1)
            move_turned(act, copy, turned_act, 3, 1)
            move_pairs(act, copy, pairs_act, 3, 1)
            relu1(3)
            relu2(3)


def first_layer_rows(nd):
    at = []
    for v in range(STEPS):
        for u, w in BLOCKS:
            m = STEPS * u + v
            for n in range(min(m, w) if m < NF else 0):
                lo, hi = sorted((ORDER[n], ORDER[m]))
                at.append((BASE[u] + n, v, hi * (hi - 1) // 2 + lo))
    return at + [(PAIRS + e, 0, NF * (NF - 1) // 2 + e) for e in range(nd)]


def kernel(**inputs):
    import numpy as np
    import concourse.bacc as bacc
    from concourse.bass_utils import run_bass_kernel_spmd

    nc = bacc.Bacc("TRN2", target_bir_lowering=False, num_devices=1)
    arrays, dram = {}, {}

    def give(name, a):
        a = np.ascontiguousarray(a)
        arrays[f"in_{name}_dram"] = a
        dram[name] = nc.dram_tensor(f"in_{name}_dram", a.shape, mybir.dt.from_np(a.dtype), kind="ExternalInput").ap()

    for name, a in inputs.items():
        if name not in ("W_top1", "b_top1"):
            give(name, a)
    w1 = np.asarray(inputs["W_top1"])
    nd = inputs["dense_ctx"].shape[1]
    steps = np.zeros((PAIRS + nd + 1, STEPS, w1.shape[1]), w1.dtype)
    part, step, row = np.array(first_layer_rows(nd)).T
    steps[part, step] = w1[row]
    steps[-1, 0] = inputs["b_top1"]
    give("w1_steps", steps)

    batch = inputs["ids"].shape[0]
    out = nc.dram_tensor("out_0_dram", (batch, 1), F32, kind="ExternalOutput").ap()
    dlrm_tower(nc, dram["dense_ctx"], dram["ids"], [dram[f"tbl_{f}"] for f in range(NF)], dram["w1_steps"],
               dram["W_top2"], dram["b_top2"], dram["W_top3"], out)
    r = run_bass_kernel_spmd(nc, [arrays], core_ids=[0])
    return r.results[0]["out_0_dram"]
```
